# Optimizing a Trainium2 kernel written in Bass

```python
import numpy as np
import jax
import jax.numpy as jnp

def _softmax(x, axis=-1):
    return jax.nn.softmax(x, axis=axis)

def _gelu(x):
    return jax.nn.gelu(x, approximate=True)

def _silu(x):
    return jax.nn.silu(x)

def _sigmoid(x):
    return jax.nn.sigmoid(x)

def _layernorm(x, axis=-1, eps=1e-05):
    m = jnp.mean(x, axis=axis, keepdims=True)
    v = jnp.var(x, axis=axis, keepdims=True)
    return (x - m) / jnp.sqrt(v + eps)

def _scatter_add(tgt, idx, src, axis=0):
    return tgt.at[idx].add(src)

def _segment_sum(src, seg, n):
    return jax.ops.segment_sum(src, seg, n)
kernel_name = 'mk_gnn_ffn_d1_gnn_r32_28a0b5'

def setup_inputs(seed: int=0):
    np.random.seed(seed)
    _w = jnp.asarray

    def _rec_inputs():
        import jax
        import jax.numpy as jnp
        _gk = jax.random.key(seed)
        x = -0.0003713 + 1 * jax.random.normal(jax.random.fold_in(_gk, 1), (50000, 256), jnp.float32)
        src = jax.random.randint(jax.random.fold_in(_gk, 2), (50000,), 0, 50000, jnp.int32)
        dst = jax.random.randint(jax.random.fold_in(_gk, 3), (50000,), 0, 50000, jnp.int32)
        _o = jnp.argsort(dst, stable=True)
        src = src[_o]
        dst = dst[_o]
        return (x, src, dst)
    x, src, dst = _rec_inputs()

    def _L0_gnn_setup():
        import jax, jax.numpy as jnp
        import numpy as np
        N_NODES = 50000
        N_EDGES = 25000
        D = 256

        def _mean_aggregate(x, src, tgt, num_nodes):
            summed = jax.ops.segment_sum(x[src], tgt, num_segments=num_nodes)
            count = jax.ops.segment_sum(jnp.ones((src.shape[0],), x.dtype), tgt, num_segments=num_nodes)
            return summed / jnp.maximum(count, 1.0)[:, None]

        def _sage_conv(x, src, tgt, W_l, b, W_r):
            agg = _mean_aggregate(x, src, tgt, x.shape[0])
            return agg @ W_l + b + x @ W_r
        key = jax.random.key(seed)
        ks = jax.random.split(key, 8)
        s = 1.0 / np.sqrt(D)
        x = jax.random.normal(ks[0], (N_NODES, D), dtype=jnp.float32)
        edge_index = jax.random.randint(ks[1], (2, N_EDGES), 0, N_NODES, dtype=jnp.int64)
        return {'x': x, 'edge_index': edge_index, 'W1_l': jax.random.normal(ks[2], (D, D), dtype=jnp.float32) * s, 'b1': jnp.zeros((D,), dtype=jnp.float32), 'W1_r': jax.random.normal(ks[3], (D, D), dtype=jnp.float32) * s, 'W2_l': jax.random.normal(ks[4], (D, D), dtype=jnp.float32) * s, 'b2': jnp.zeros((D,), dtype=jnp.float32), 'W2_r': jax.random.normal(ks[5], (D, D), dtype=jnp.float32) * s}
    _L0_gnn_all = _L0_gnn_setup()
    _L0_gnn_in = {k: v for k, v in _L0_gnn_all.items() if k in ('W1_l', 'b1', 'W1_r', 'W2_l', 'b2', 'W2_r')}
    del _L0_gnn_all

    def _L0_ffn_setup():
        import jax, jax.numpy as jnp
        import numpy as np
        B, S, D = (8, 128, 256)
        H = 4 * D
        CAPACITY = 0.5
        key = jax.random.key(seed)
        ks = jax.random.split(key, 6)
        x = jax.random.normal(ks[0], (B, S, D), dtype=jnp.float32)
        attention_mask = jnp.zeros((B, 1, 1, S), dtype=jnp.float32)
        wr = jax.random.normal(ks[1], (D, 1), dtype=jnp.float32) * 0.02
        br = jnp.zeros((1,), dtype=jnp.float32)
        w1 = jax.random.normal(ks[2], (D, H), dtype=jnp.float32) * 0.02
        b1 = jnp.zeros((H,), dtype=jnp.float32)
        w2 = jax.random.normal(ks[3], (H, D), dtype=jnp.float32) * 0.02
        b2 = jnp.zeros((D,), dtype=jnp.float32)
        return {'x': x, 'attention_mask': attention_mask, 'wr': wr, 'br': br, 'w1': w1, 'b1': b1, 'w2': w2, 'b2': b2}
    _L0_ffn_all = _L0_ffn_setup()
    _L0_ffn_in = {k: v for k, v in _L0_ffn_all.items() if k in ('attention_mask', 'wr', 'br', 'w1', 'b1', 'w2', 'b2')}
    del _L0_ffn_all
    return {'x': x, 'src': src, 'dst': dst, 'L0_gnn_W1_l': _L0_gnn_in['W1_l'], 'L0_gnn_b1': _L0_gnn_in['b1'], 'L0_gnn_W1_r': _L0_gnn_in['W1_r'], 'L0_gnn_W2_l': _L0_gnn_in['W2_l'], 'L0_gnn_b2': _L0_gnn_in['b2'], 'L0_gnn_W2_r': _L0_gnn_in['W2_r'], 'L0_ffn_attention_mask': _L0_ffn_in['attention_mask'], 'L0_ffn_wr': _L0_ffn_in['wr'], 'L0_ffn_br': _L0_ffn_in['br'], 'L0_ffn_w1': _L0_ffn_in['w1'], 'L0_ffn_b1': _L0_ffn_in['b1'], 'L0_ffn_w2': _L0_ffn_in['w2'], 'L0_ffn_b2': _L0_ffn_in['b2']}

def reference(x, src, dst, L0_gnn_W1_l, L0_gnn_b1, L0_gnn_W1_r, L0_gnn_W2_l, L0_gnn_b2, L0_gnn_W2_r, L0_ffn_attention_mask, L0_ffn_wr, L0_ffn_br, L0_ffn_w1, L0_ffn_b1, L0_ffn_w2, L0_ffn_b2):
    import jax
    import jax.numpy as jnp

    def _L0_gnn_ref(x, edge_index, W1_l, b1, W1_r, W2_l, b2, W2_r):
        import jax, jax.numpy as jnp
        import numpy as np
        N_NODES = 50000
        N_EDGES = 25000
        D = 256

        def _mean_aggregate(x, src, tgt, num_nodes):
            summed = jax.ops.segment_sum(x[src], tgt, num_segments=num_nodes)
            count = jax.ops.segment_sum(jnp.ones((src.shape[0],), x.dtype), tgt, num_segments=num_nodes)
            return summed / jnp.maximum(count, 1.0)[:, None]

        def _sage_conv(x, src, tgt, W_l, b, W_r):
            agg = _mean_aggregate(x, src, tgt, x.shape[0])
            return agg @ W_l + b + x @ W_r
        src, tgt = (edge_index[0], edge_index[1])
        h = jax.nn.relu(_sage_conv(x, src, tgt, W1_l, b1, W1_r))
        return _sage_conv(h, src, tgt, W2_l, b2, W2_r)

    def _L0_ffn_ref(x, attention_mask, wr, br, w1, b1, w2, b2):
        import jax, jax.numpy as jnp
        import numpy as np
        B, S, D = (8, 128, 256)
        H = 4 * D
        CAPACITY = 0.5
        b, s, d = x.shape
        weights = (jnp.einsum('bsd,do->bso', x, wr) + br)[..., 0]
        k = max(1, int(CAPACITY * s))
        kk = k - 1 if k > 1 else 1
        _, idx = jax.lax.top_k(weights, k)
        sel_idx = idx[:, :kk]
        sel = jnp.take_along_axis(x, sel_idx[:, :, None], axis=1)
        h = jax.nn.gelu(jnp.einsum('bkd,dh->bkh', sel, w1) + b1)
        y = jnp.einsum('bkh,hd->bkd', h, w2) + b2
        w_sel = jnp.take_along_axis(weights, sel_idx, axis=1)
        y = y * w_sel[..., None]
        batch_idx = jnp.arange(b)[:, None]
        processed = jnp.zeros_like(x).at[batch_idx, sel_idx].set(y)
        return processed + x
    edge_index = jnp.stack([src, dst])
    x = x + _L0_gnn_ref(_layernorm(x, axis=-1), edge_index, L0_gnn_W1_l, L0_gnn_b1, L0_gnn_W1_r, L0_gnn_W2_l, L0_gnn_b2, L0_gnn_W2_r)
    x = x + _L0_ffn_ref(_layernorm(x, axis=-1)[None], L0_ffn_attention_mask, L0_ffn_wr, L0_ffn_br, L0_ffn_w1, L0_ffn_b1, L0_ffn_w2, L0_ffn_b2)[0]
    return x

_drawn_inputs = setup_inputs


def setup_inputs(seed=0):
    import zlib

    import numpy as np

    out = dict(_drawn_inputs(seed))
    spreads = {'L0_gnn_b1': (0.0, 0.1),
     'L0_gnn_b2': (0.0, 0.1),
     'L0_ffn_b1': (0.0, 0.8),
     'L0_ffn_b2': (0.0, 0.8)}
    factors = {'L0_ffn_wr': 3.706, 'L0_ffn_w1': 8.0, 'L0_ffn_w2': 8.0}
    for name, (base, spread) in spreads.items():
        noise = np.random.default_rng([zlib.crc32(name.encode()), seed]).standard_normal(out[name].shape)
        drawn = base * np.exp(spread * noise) if base else spread * noise
        out[name] = jnp.asarray(drawn.astype(out[name].dtype))
    for name, factor in factors.items():
        out[name] = (out[name] * factor).astype(out[name].dtype)
    return out
```

```python
import concourse.bass as bass
from concourse import mybir
from contextlib import ExitStack


def gnn_ffn_kernel(nc, x, src, dst, W1_l, b1, W1_r, W2_l, b2, W2_r, wr, br, F1, fb1, F2, fb2, out):
    fp32, f32r = mybir.dt.float32, mybir.dt.float32r
    i32, u32 = mybir.dt.int32, mybir.dt.uint32
    ALU, ACT, AX = mybir.AluOpType, mybir.ActivationFunctionType, mybir.AxisListType
    ds = bass.ds

    N, D = x.shape
    E = dst.shape[0]
    H = F1.shape[1]
    P = 128
    KD, KH = D // P, H // P
    R, TN = 125, 4
    GN = R * TN
    NG = N // GN
    NE, TE, EC = 100, 5, P
    NT = N // NE
    NC = N // R
    EPS = 1e-5
    KSEL = N // 2 - 1
    EB = E // R
    OCT = 8
    MAIN_OCTS = -(-KSEL // (R * OCT))
    MAIN = MAIN_OCTS * OCT
    REST_OCTS = -(-(KSEL // NC + 1) * (NC - MAIN) // (R * OCT))
    OVER_OCTS = 5
    OVER = OVER_OCTS * OCT
    OVER_MAX = -(-(NC - MAIN) // OVER)
    FAR = 1.0e6
    HALF_BITS = 16
    DIGITS = HALF_BITS // 2

    rec = nc.dram_tensor("edge_records", [2 * E + 2 * EC, 4], fp32).ap()
    h_dram = nc.dram_tensor("hidden", [N, D], fp32).ap()
    ends_dram = nc.dram_tensor("run_ends", [5, R], fp32).ap()
    carry_dram = nc.dram_tensor("run_carries", [2, R], fp32).ap()
    lo_dram = nc.dram_tensor("tile_starts", [NT], i32).ap()
    rest_dram = nc.dram_tensor("rest_rows", [(REST_OCTS + 1) * OCT * R, 2], i32).ap()
    stat_dram = nc.dram_tensor("row_stats", [N, 4], fp32).ap()

    ctx = ExitStack()
    with ctx:
        def sb(name, shape, dt=fp32):
            return ctx.enter_context(nc.sbuf_tensor("sb_" + name, shape, dt))

        def sems(prefix, names):
            return {n: ctx.enter_context(nc.semaphore(prefix + n)) for n in names.split()}

        ident, ones = sb("ident", [P, P]), sb("ones", [P, P])
        ones_r = sb("ones_r", [2, P], f32r)
        iota_n, tile_base = sb("iota_n", [P, GN]), sb("tile_base", [P, NT])
        tri = sb("tri", [R, R])
        col_rank = sb("col_rank", [R, NC])
        lane = sb("lane", [R, 2])
        eps_col = sb("eps_col", [P, 1])
        pool_scrap, dve_scrap = sb("pool_scrap", [1, 1]), sb("dve_scrap", [1, 1])
        stage = sb("stage", [P, KH * D])
        convs = ("w1l", "w1r", "w2l", "w2r")
        w_hi = {n: sb(n + "_hi", [P, KD, D], f32r) for n in convs}
        w_lo = {n: sb(n + "_lo", [P, KD, D], f32r) for n in convs}
        f1_hi, f1_lo = sb("f1_hi", [P, KD, H], f32r), sb("f1_lo", [P, KD, H], f32r)
        f2_hi, f2_lo = sb("f2_hi", [P, KH, D], f32r), sb("f2_lo", [P, KH, D], f32r)
        bias_in = sb("bias_in", [2, 3, D])
        bias_h = sb("bias_h", [2, 3, D])
        bias_hi = sb("bias_hi", [2, 3, D], f32r)
        bias_r = sb("bias_r", [2, 3, D], f32r)
        fb1_col = sb("fb1_col", [P, KH])
        wr_row, br_col = sb("wr_row", [R, D]), sb("br_col", [R, 1])
        edge_tab = sb("edge_tab", [P, NT, 4])
        pad_rec = sb("pad_rec", [EC, 4])
        lo_row = sb("lo_row", [1, NT], i32)
        stat = sb("stat", [R, NC, 4])
        X, XN = sb("X", [P, 2, TN, D]), sb("XN", [P, 2, TN, D])
        G, GB = sb("G", [P, 2, TE, D]), sb("GB", [P, 2, TE, D])
        O = sb("O", [R, 2, TN, D])
        S = sb("S", [P, 2, TE, NE])
        idx = sb("idx", [P, 2, TE], u32)
        edge_at = sb("edge_at", [P, 2, TE])
        ST, MV = sb("ST", [P, 2, TN + TE, 6]), sb("MV", [P, 2, TN + TE, 2])
        RT, RR, RP, NMR = (sb(n, [P, 2, TN + TE]) for n in ("RT", "RR", "RP", "NMR"))
        wdot = sb("wdot", [R, 2, TN])
        U = sb("U", [P, 4 * 2 * KD * GN], f32r)
        part = 2 * KD * GN
        XTH, XTL, ATH, ATL = (U[:, n * part:(n + 1) * part].rearrange("p (s k n) -> p s k n", s=2, k=KD)
                              for n in range(4))
        HTH, HTL = (U[:, n * KH * GN:(n + 1) * KH * GN].rearrange("p (h n) -> p h n", h=KH) for n in range(2))
        CTH, CTL = sb("CTH", [P, KD, GN], f32r), sb("CTL", [P, KD, GN], f32r)
        GL = sb("GL", [P, 2, GN])
        BG, X2, YO = X[0:R], XN[0:R], G[0:R, :, 0:TN, :]
        SG = sb("SG", [R, 2, TN, 4])
        ig, iq, isc = (sb(n, [R, 2, TN], u32) for n in ("ig", "iq", "isc"))
        m8, m8far = sb("m8", [R, OCT]), sb("m8far", [R, OCT])
        n_tab, q_tab = (sb(n, [R, (MAIN_OCTS + REST_OCTS + 1) * OCT], u32) for n in ("n_tab", "q_tab"))
        over_rows, over_at = sb("over_rows", [R, OVER, 2], u32), sb("over_at", [R, OVER], u32)
        over_cnt, over_first = sb("over_cnt", [R, 1]), sb("over_first", [R, 1])
        found, digit, lane_cnt, need = (sb(n, [R, 1]) for n in ("found", "digit", "lane_cnt", "need"))
        trial, reach, lane_cnt3 = (sb(n, [R, 3]) for n in ("trial", "reach", "lane_cnt3"))
        steps = [sb(f"steps{n}", [R, 3]) for n in range(2)]
        lane_max, oct_f, over_f = (sb(n, [1, 1]) for n in ("lane_max", "oct_f", "over_f"))
        rest_f, steps_f = sb("rest_f", [1, REST_OCTS]), sb("steps_f", [1, OVER_MAX])
        oct_n, over_n = sb("oct_n", [1, 1], i32), sb("over_n", [1, 1], i32)
        run_end = sb("run_end", [R, 5])
        run_row, carry_row, scan_row = sb("run_row", [1, 5, R]), sb("carry_row", [1, 2, R]), sb("scan_row", [1, 2, R])
        carry_in = sb("carry_in", [R, 2])
        blk_last_i, blk_last = sb("blk_last_i", [1, R], i32), sb("blk_last", [1, R])
        near_i, near = sb("near_i", [R, 2], i32), sb("near", [R, 2])
        thr, blk_f, blk_cnt, lo_f = (sb(n, [R, TN]) for n in ("thr", "blk_f", "blk_cnt", "lo_f"))
        blk_u, lo_i = sb("blk_u", [R, TN], u32), sb("lo_i", [R, TN], i32)
        CH_MAX = -(-E // EC)
        bound, tile_cnt = sb("bound", [1, NT + 1]), sb("tile_cnt", [1, NT])
        grp = [sb(f"grp{n}", [1, NG]) for n in range(7)]
        ordered, unordered, all_edges, fix_sum = (sb(n, [1, 1]) for n in ("ordered", "unordered", "all_edges", "fix_sum"))
        fix_start, fix_chunks, fix_before = (sb(n, [1, NG], i32) for n in ("fix_start", "fix_chunks", "fix_before"))
        fix_list, fix_num = sb("fix_list", [1, NG], i32), sb("fix_num", [1, 1], i32)
        place, place_col = sb("place", [1, NG]), sb("place_col", [NG, 1])
        fix_rec = sb("fix_rec", [EC, 4])
        fix_sums = stage[:, 0:(KD + 1) * GN].rearrange("p (d n) -> p d n", d=KD + 1)
        WIDE = NC + 1

        def wides(t, n, dt=fp32):
            flat = t[0:R].rearrange("p s k d -> p (s k d)")
            return [flat[:, i * WIDE:i * WIDE + NC] for i in range(n)]

        wx, wxn, wg, wgb = wides(X, 5), wides(XN, 5), wides(G, 6), wides(GB, 6)
        place_at = GB[0:NG].rearrange("p s k d -> p (s k d)")[:, 0:NG]
        no_row = wgb[5].bitcast(i32)
        goes_on = XN[0:R].rearrange("p s k d -> p (s k d)")[:, 0:WIDE]
        banks = [ctx.enter_context(nc.psum_tensor(f"ps_{i}", [P, 512], fp32)) for i in range(8)]

        q = sems("q_", "dst_in src_in near_in pool_step pool_const bias_ld w_ld w_hi w_lo ends dram_out ends_in carries "
                       "rest_set rest_out fix_ok fix_ga place listed carry_ld blk_last_ok blk_all blk_idx row_in lo_done lo_in rec_done rec_out dve_step near_set waited")
        a = sems("a_", "x0 x1 rec0 rec1 rec2 rec3 st0 st1 ga0 ga1 idx stats aggr sqrt rstd nmr nme xn gn S T A D hi lo h")
        fix_names = "done free rec idx in step aggr sqrt op sums rows row_step row_aggr row_sqrt row_in T lo D res st landed"
        fa, fb = sems("fa_", fix_names), sems("fb_", fix_names)
        b = sems("b_", "h0 h1 x0 x1 ga0 ga1 st0 st1 idx S Sw T A D hi lo x1s stats aggr sqrt rstd nmr dot prod tab base")
        c = sems("c_", "step counted total cand octs over8 over rest_in stat_done stat_out max8 tab8 idx sidx g0 g1 sc0 sc1 "
                       "x2 T hiT loT h1 gelu hhi hlo m2a m2b y")
        ctx.enter_context(nc.allow_non_contiguous_dma(reason="a few columns of the set-up"))
        block = ctx.enter_context(nc.Block())

        def rows_of(t, g):
            return t.rearrange("(g k p) d -> g p k d", k=TN, p=R)[ds(g, 1)].rearrange("g p k d -> (g p) k d")

        def operand(e, n):
            own = (n < KD) == (e is b)
            return own, n % KD, n % KD + (0 if own else KD)

        dst_blk, src_blk = (t.rearrange("(p j) -> p j", p=R) for t in (dst, src))
        dst_i, src_i = wx[0].bitcast(i32), wx[1].bitcast(i32)
        flat = "p k n -> p (k n)"
        weights = [(w, KD, stage[:, n * KD * D:(n + 1) * KD * D], w_hi[c], w_lo[c])
                   for n, (c, w) in enumerate(zip(convs, (W1_l, W1_r, W2_l, W2_r)))]
        weights += [(F1, KD, stage[:, :], f1_hi, f1_lo), (F2, KH, stage[:, :], f2_hi, f2_lo)]

        @block.sync
        def _(sp):
            sp.dma_start(dst_i, dst_blk).then_inc(q["dst_in"], 16)
            sp.dma_start(src_i, src_blk).then_inc(q["src_in"], 16)
            sp.wait_ge(q["near_set"], 1)
            sp.dma_start(near_i[1:R, 0:1], dst_blk[0:R - 1, EB - 1:EB]).then_inc(q["near_in"], 16)
            sp.dma_start(near_i[0:R - 1, 1:2], dst_blk[1:R, 0:1]).then_inc(q["near_in"], 16)
            sp.dma_start(blk_last_i[:, :], dst_blk[:, EB - 1:EB].rearrange("p a -> a p")).then_inc(q["near_in"], 16)
            sp.wait_ge(q["ends"], 1)
            sp.dma_start(ends_dram.rearrange("c p -> p c"), run_end[:, :]).then_inc(q["dram_out"], 16)
            sp.wait_ge(q["dram_out"], 16)
            sp.dma_start(run_row[:, :, :], ends_dram[None, :, :]).then_inc(q["ends_in"], 16)
            sp.wait_ge(q["carries"], 1)
            sp.dma_start(carry_dram[None, :, :], carry_row[:, :, :]).then_inc(q["dram_out"], 16)
            sp.wait_ge(q["dram_out"], 32)
            sp.dma_start(carry_in[:, :], carry_dram.rearrange("c p -> p c")).then_inc(q["carry_ld"], 16)
            sp.wait_ge(q["rec_done"], 1)
            sp.dma_start(rec[0:E, :].rearrange("(p j) w -> p j w", p=R), stat[:, :, :]).then_inc(q["rec_out"], 16)
            sp.dma_start(rec[E:E + EC, :], pad_rec[:, :]).then_inc(q["rec_out"], 16)
            sp.wait_ge(q["rest_set"], 1)
            sp.dma_start(rest_dram.rearrange("(p a) w -> p (a w)", p=R),
                         no_row[:, 0:2 * (REST_OCTS + 1) * OCT]).then_inc(q["rest_out"], 16)
            sp.wait_ge(q["lo_done"], 1)
            sp.dma_start(lo_dram.rearrange("(p k) -> p k", k=TN), lo_i[:, :]).then_inc(q["dram_out"], 16)
            sp.wait_ge(q["dram_out"], 48)
            sp.dma_start(lo_row[:, :], lo_dram[None, :]).then_inc(q["lo_in"], 16)
            sp.wait_ge(q["rest_out"], 16)
            sp.wait_ge(q["rec_out"], 32)
            sp.wait_ge(q["lo_in"], 16)

            def load_x(g, s, first):
                if not first:
                    sp.wait_ge(a["xn"], g - 1)
                sp.dma_start(X[0:R, s], rows_of(x, g)).then_inc(a[f"x{s}"], 16)

            def load_records(g, s4):
                _, starts = nc.values_load_multi_w_load_instructions(lo_row[0:1, ds(TE * g, TE)], engines=[mybir.EngineType.SP],
                                                                     min_val=0, max_val=E)
                for j, start in enumerate(starts):
                    sp.dma_start(edge_tab[:, ds(TE * g + j, 1), :].rearrange("p a w -> p (a w)"),
                                 rec[ds(start, EC), :]).then_inc(a[f"rec{s4}"], 16)

            def store_h(g, s):
                sp.wait_ge(a["h"], g + 1)
                sp.dma_start(rows_of(h_dram, g), O[:, s]).then_inc(a[f"st{s}"], 16)

            for g in range(4):
                load_records(g, g)
                if g < 2:
                    load_x(g, g, True)
            for g in range(4):
                load_x(g + 2, g % 2, False)
                if g >= 3:
                    store_h(g - 3, (g - 3) % 2)
                load_records(g + 4, g)
            with sp.Fori(1, NG // 4 - 1) as i:
                for n in range(4):
                    load_x(4 * i + n + 2, n % 2, False)
                    store_h(4 * i + n - 3, (n + 1) % 2)
                    load_records(4 * i + n + 4, n)
            for g in range(NG - 4, NG + 3):
                if g + 2 < NG:
                    load_x(g + 2, g % 2, False)
                store_h(g - 3, (g - 3) % 2)
            for s in range(2):
                sp.wait_ge(a[f"st{s}"], 16 * (NG // 2))

            def repair(f, second):
                sp.wait_ge(q["fix_ok"], 1)
                num = sp.value_load(fix_num[0:1, 0:1], min_val=0, max_val=NG)
                with sp.If(num > 0):
                    with sp.Fori(0, num) as k:
                        g = sp.value_load(fix_list[0:1, ds(k, 1)], min_val=0, max_val=NG - 1)
                        start = sp.value_load(fix_start[0:1, ds(g, 1)], min_val=0, max_val=E)
                        chunks = sp.value_load(fix_chunks[0:1, ds(g, 1)], min_val=1, max_val=CH_MAX)
                        before = sp.value_load(fix_before[0:1, ds(g, 1)], min_val=0, max_val=NG * CH_MAX)
                        sp.dma_start(X[0:R, 0], rows_of(x, g)).then_inc(f["rows"], 16)
                        sp.dma_start(XN[0:R, 0], rows_of(h_dram if second else x, g)).then_inc(f["rows"], 16)
                        with sp.Fori(0, chunks) as j:
                            sp.wait_ge(f["free"], before + j + 1)
                            sp.dma_start(fix_rec[:, :], rec[ds(start + EC * j, EC), :]).then_inc(f["rec"], 16)
                        sp.wait_ge(f["res"], k + 1)
                        sp.dma_start(rows_of(out if second else h_dram, g), O[:, 0]).then_inc(f["st"], 16)
                        sp.wait_ge(f["st"], 16 * k + 16)
                        sp.sem_inc(f["landed"], 1)
                sp.sem_inc(f["done"], 1)

            repair(fa, False)

            def load_h(g, s, first):
                if not first:
                    sp.wait_ge(b["T"], 2 * g - 2)
                sp.dma_start(XN[0:R, s], rows_of(h_dram, g)).then_inc(b[f"h{s}"], 16)

            def load_xb(g, s, first):
                if not first:
                    sp.wait_ge(b["base"], g - 1)
                    sp.wait_ge(b["dot"], g - 1)
                sp.dma_start(X[0:R, s], rows_of(x, g)).then_inc(b[f"x{s}"], 16)

            def store_base(g, s):
                sp.wait_ge(b["base"], g + 1)
                sp.dma_start(rows_of(out, g), O[:, s]).then_inc(b[f"st{s}"], 16)

            for g in range(2):
                load_h(g, g, True)
                load_xb(g, g, True)
            for g in range(4):
                load_h(g + 2, g % 2, False)
                if g == 3:
                    store_base(0, 0)
                    load_xb(2, 0, False)
            with sp.Fori(2, NG // 2 - 1) as i:
                for s in range(2):
                    load_h(2 * i + s + 2, s, False)
                    store_base(2 * i + s - 3, 1 - s)
                    load_xb(2 * i + s - 1, 1 - s, False)
            for g in range(NG - 2, NG + 3):
                store_base(g - 3, (g - 3) % 2)
                if g - 1 < NG:
                    load_xb(g - 1, (g - 1) % 2, False)
            for s in range(2):
                sp.wait_ge(b[f"st{s}"], 16 * (NG // 2))
            repair(fb, True)

            sp.wait_ge(c["stat_done"], 1)
            sp.dma_start(stat_dram.rearrange("(p c) w -> p c w", p=R), stat[:, :, :]).then_inc(c["stat_out"], 16)
            sp.wait_ge(c["stat_out"], 16)
            sp.wait_ge(c["octs"], 1)
            octs = sp.value_load(oct_n[0:1, 0:1], min_val=MAIN_OCTS + 1, max_val=MAIN_OCTS + REST_OCTS)
            overs = sp.value_load(over_n[0:1, 0:1], min_val=1, max_val=OVER_MAX)
            sp.wait_ge(c["over"], 16 * OVER * overs)
            sp.sem_inc(q["waited"], 1)
            with sp.Fori(MAIN_OCTS, octs + 1) as m:
                for w, tab in enumerate((n_tab, q_tab)):
                    rows = rest_dram.rearrange("(m c p) w -> m p c w", c=OCT, p=R)[ds(m - MAIN_OCTS, 1), :, :, w]
                    sp.dma_start(tab[:, ds(OCT * m, OCT)], rows.rearrange("m p c -> (m p) c").bitcast(u32)).then_inc(c["rest_in"], 16)
                sp.wait_ge(c["rest_in"], 32 * (m - (MAIN_OCTS - 1)))
                sp.sem_inc(q["waited"], 1)

        @block.gpsimd
        def _(pool):
            gp = nc.gpsimd

            def wait_apart(done, count):
                pool.wait_ge(done, count)
                gp.tensor_tensor(pool_scrap[:, :], ones[0:1, 0:1], ones[0:1, 0:1], ALU.mult)

            def iota(t, pattern, base, mult):
                return gp.iota(t, pattern, base=base, channel_multiplier=mult, allow_small_or_imprecise_dtypes=True)

            gp.memset(ident[:, :], 0.0)
            gp.memset(tri[:, :], 1.0).then_inc(q["pool_step"], 1)
            pool.wait_ge(q["pool_step"], 1)
            gp.affine_select(out=ident[:, :], in_=ident[:, :], compare_op=ALU.not_equal, fill=1.0, base=0,
                             pattern=[[-1, P]], channel_multiplier=1)
            gp.affine_select(out=tri[:, :], in_=tri[:, :], compare_op=ALU.is_gt, fill=0.0, base=0,
                             pattern=[[1, R]], channel_multiplier=-1)
            gp.memset(ones[:, :], 1.0)
            iota(thr[:, :], [[NE, TN]], 0, NE * TN)
            iota(iota_n[:, :], [[1, GN]], 0, 0)
            iota(tile_base[:, :], [[NE, NT]], 0, 0)
            iota(col_rank[:, :], [[-1, NC]], NC, 0)
            iota(lane[:, 0:1], [[0, 1]], N, 1)
            iota(lane[:, 1:2], [[0, 1]], NC, NC).then_inc(q["pool_const"], 1)
            for n, t in enumerate((b1, b2, fb2)):
                gp.dma_start(bias_in[:, n, :], t.rearrange("(a d) -> a d", a=1).broadcast_to([2, D])).then_inc(q["bias_ld"], 16)
            gp.dma_start(fb1_col[:, :], fb1.rearrange("(h p) -> p h", p=P)).then_inc(q["bias_ld"], 16)
            gp.dma_start(wr_row[:, :], wr.rearrange("d a -> a d").broadcast_to([R, D])).then_inc(q["bias_ld"], 16)
            gp.dma_start(br_col[:, :], br.rearrange("(a d) -> a d", a=1).broadcast_to([R, 1])).then_inc(q["bias_ld"], 16)
            pool.wait_ge(q["blk_idx"], 1)
            for k in range(TN):
                gp.indirect_dma_start(out=wg[k].bitcast(i32), out_offset=None, in_=dst_blk,
                                      in_offset=bass.IndirectOffsetOnAxis(ap=blk_u[:, k:k + 1], axis=0),
                                      bounds_check=R - 1, oob_is_err=False).then_inc(q["row_in"], 16)

            def fetch(out_t, table, offsets, done):
                for j in range(offsets.shape[1]):
                    gp.indirect_dma_start(out=out_t[:, j], out_offset=None, in_=table,
                                          in_offset=bass.IndirectOffsetOnAxis(ap=offsets[:, j:j + 1], axis=0),
                                          bounds_check=N - 1, oob_is_err=False).then_inc(done, 16)

            def edge_sources(g, s, done):
                gp.tensor_copy(idx[:, s, :], edge_tab[:, ds(TE * g, TE), 0].bitcast(i32)).then_inc(done, 1)
                wait_apart(done, g + 1)

            def gather_x(g, s4, turn, first):
                pool.wait_ge(a[f"rec{s4}"], 16 * TE * (turn + 1))
                if not first:
                    pool.wait_ge(a["gn"], g - 1)
                edge_sources(g, s4 % 2, a["idx"])
                fetch(G[:, s4 % 2], x, idx[:, s4 % 2], a[f"ga{s4 % 2}"])

            gather_x(0, 0, 0, True)
            for g in range(1, 4):
                gather_x(g, g, 0, g < 2)
            with pool.Fori(1, NG // 4) as i:
                for s4 in range(4):
                    gather_x(4 * i + s4, s4, i, False)

            def repair(f, second):
                pool.wait_ge(q["fix_ok"], 1)
                num = pool.value_load(fix_num[0:1, 0:1], min_val=0, max_val=NG)
                with pool.If(num > 0):
                    with pool.Fori(0, num) as k:
                        g = pool.value_load(fix_list[0:1, ds(k, 1)], min_val=0, max_val=NG - 1)
                        chunks = pool.value_load(fix_chunks[0:1, ds(g, 1)], min_val=1, max_val=CH_MAX)
                        before = pool.value_load(fix_before[0:1, ds(g, 1)], min_val=0, max_val=NG * CH_MAX)
                        with pool.Fori(0, chunks) as j:
                            pool.wait_ge(f["rec"], 16 * (before + j) + 16)
                            pool.sem_inc(q["waited"], 1)
                            gp.tensor_copy(idx[:, 0, 0:1], fix_rec[:, 0:1].bitcast(i32)).then_inc(f["idx"], 1)
                            pool.wait_ge(f["idx"], before + j + 1)
                            pool.sem_inc(q["waited"], 1)
                            fetch((GB if second else G)[:, 0], h_dram if second else x, idx[:, 0, 0:1], q["fix_ga"])
                            pool.wait_ge(q["fix_ga"], 16)
                            gp.inc_swdge_sem([q["fix_ga"]], [16], mode="sub")
                            pool.sem_inc(f["in"], 1)
                pool.wait_ge(f["done"], 1)

            repair(fa, False)
            for s in range(2):
                pool.wait_ge(a[f"st{s}"], 16 * (NG // 2))

            def gather_h(g, s, first):
                if not first:
                    pool.wait_ge(b["A"], 2 * g - 2)
                edge_sources(g, s, b["idx"])
                fetch(GB[:, s], h_dram, idx[:, s], b[f"ga{s}"])

            for g in range(4):
                gather_h(g, g % 2, g < 2)
            with pool.Fori(2, NG // 2) as i:
                for s in range(2):
                    gather_h(2 * i + s, s, False)
            repair(fb, True)

            def fetch_selected(n, s, octs_made, first, rest=False):
                pool.wait_ge(c["rest_in" if rest else "tab8"], 32 * octs_made if rest else octs_made)
                if not first:
                    pool.wait_ge(c["y"], 2 * n - 2)
                gp.tensor_copy(ig[:, s, :], n_tab[:, ds(TN * n, TN)])
                gp.tensor_copy(iq[:, s, :], q_tab[:, ds(TN * n, TN)]).then_inc(c["idx"], 1)
                wait_apart(c["idx"], n + 1)
                fetch(SG[:, s], stat_dram, iq[:, s], c[f"g{s}"])
                fetch(BG[:, s], out, ig[:, s], c[f"g{s}"])

            def store_selected(done, s):
                pool.wait_ge(c["y"], 2 * done)
                gp.tensor_copy(isc[:, s, :], n_tab[:, ds(TN * done - TN, TN)]).then_inc(c["sidx"], 1)
                wait_apart(c["sidx"], done)
                for k in range(TN):
                    gp.indirect_dma_start(out=out, out_offset=bass.IndirectOffsetOnAxis(ap=isc[:, s, k:k + 1], axis=0),
                                          in_=YO[:, s, k, :], in_offset=None,
                                          bounds_check=N - 1, oob_is_err=False).then_inc(c[f"sc{s}"], 16)

            def list_over(made):
                for k in range(OCT * made.start, OCT * made.stop):
                    gp.indirect_dma_start(out=rest_dram, out_offset=bass.IndirectOffsetOnAxis(ap=over_at[:, k:k + 1], axis=0),
                                          in_=over_rows[:, k, :], in_offset=None,
                                          bounds_check=(REST_OCTS + 1) * OCT * R - 1, oob_is_err=False).then_inc(c["over"], 16)

            pool.wait_ge(c["stat_out"], 16)
            fetch_selected(0, 0, 1, True)
            fetch_selected(1, 1, 1, True)
            pool.wait_ge(q["rest_out"], 16)
            for m in range(OVER_OCTS - 2):
                pool.wait_ge(c["over8"], 3 * m + 3)
                list_over(range(m, m + 1))
            fetch_selected(2, 0, 2, False)
            pool.wait_ge(c["over8"], 3 * OVER_OCTS)
            list_over(range(OVER_OCTS - 2, OVER_OCTS))
            pool.wait_ge(c["octs"], 1)
            octs = pool.value_load(oct_n[0:1, 0:1], min_val=MAIN_OCTS + 1, max_val=MAIN_OCTS + REST_OCTS)
            overs = pool.value_load(over_n[0:1, 0:1], min_val=1, max_val=OVER_MAX)
            with pool.If(overs > 1):
                with pool.Fori(1, overs) as i:
                    pool.wait_ge(c["over8"], 3 * OVER_OCTS * (i + 1))
                    pool.sem_inc(q["waited"], 1)
                    list_over(range(OVER_OCTS))
            store_selected(1, 0)
            with pool.Fori(1, MAIN_OCTS - 1) as i:
                fetch_selected(2 * i + 1, 1, i + 1, False)
                store_selected(2 * i, 1)
                fetch_selected(2 * i + 2, 0, i + 2, False)
                store_selected(2 * i + 1, 0)
            with pool.Fori(MAIN_OCTS - 1, octs) as i:
                fetch_selected(2 * i + 1, 1, MAIN_OCTS, False)
                store_selected(2 * i, 1)
                fetch_selected(2 * i + 2, 0, i + (2 - MAIN_OCTS), False, True)
                store_selected(2 * i + 1, 0)
            store_selected(2 * octs, 1)
            for s in range(2):
                pool.wait_ge(c[f"sc{s}"], 16 * TN * octs)

        @block.vector
        def _(dve):
            v = nc.vector
            taken = {}

            def after(ins, on):
                taken[on.name] = taken.get(on.name, 0) + 1
                ins.then_inc(on, 1)
                dve.wait_ge(on, taken[on.name])

            def weight_low(n):
                _, _, at, hi, lo = weights[n]
                dve.wait_ge(q["w_hi"], n + 1)
                after(v.tensor_tensor(lo[:, :, :].rearrange(flat), at, hi[:, :, :].rearrange(flat).bitcast(fp32),
                                      ALU.subtract), q["w_lo"])

            st = q["dve_step"]
            v.memset(edge_tab[:, 0, :], 0.0)
            v.memset(MV[:, :, :, :], 0.0)
            v.memset(SG[:, :, :, :], 0.0)
            v.memset(eps_col[:, :], EPS)
            v.memset(pad_rec[:, :], 0.0)
            v.memset(wxn[1], 1.0)
            for k in range(TN):
                v.memset(wg[k].bitcast(i32), N)
            after(v.memset(no_row, N), q["rest_set"])
            after(v.memset(near_i[:, :], -1), q["near_set"])
            v.memset(pad_rec[:, 1:2], -FAR)
            dst_f, one, from_start, to_end, deg = wx[2], wxn[1], wxn[2], wxn[3], wxn[4]
            dve.wait_ge(q["dst_in"], 16)
            v.tensor_copy(dst_f, dst_i)
            dve.wait_ge(q["near_in"], 48)
            v.tensor_copy(blk_last[:, :], blk_last_i[:, :]).then_inc(q["blk_last_ok"], 1)
            after(v.tensor_copy(near[:, :], near_i[:, :]), st)
            v.tensor_tensor(goes_on[:, 1:EB], dst_f[:, 1:EB], dst_f[:, 0:EB - 1], ALU.is_equal)
            v.tensor_tensor(goes_on[:, 0:1], dst_f[:, 0:1], near[:, 0:1], ALU.is_equal)
            after(v.tensor_tensor(goes_on[:, EB:EB + 1], dst_f[:, EB - 1:EB], near[:, 1:2], ALU.is_equal), st)
            before, behind = goes_on[:, 0:EB], goes_on[:, 1:EB + 1]
            v.tensor_tensor_scan(from_start, before, one, 0.0, ALU.mult, ALU.add)
            v.tensor_tensor_scan(to_end[:, ::-1], behind[:, ::-1], one, 0.0, ALU.mult, ALU.add)
            v.tensor_reduce(run_end[:, 1:2], before, AX.X, ALU.min)
            v.tensor_reduce(run_end[:, 3:4], behind, AX.X, ALU.min)
            v.tensor_tensor(wgb[0][:, 1:EB], dst_f[:, 0:EB - 1], dst_f[:, 1:EB], ALU.is_le)
            after(v.tensor_tensor(wgb[0][:, 0:1], near[:, 0:1], dst_f[:, 0:1], ALU.is_le), st)
            after(v.tensor_reduce(run_end[:, 4:5], wgb[0], AX.X, ALU.min), st)
            v.tensor_copy(run_end[:, 0:1], from_start[:, EB - 1:EB])
            after(v.tensor_copy(run_end[:, 2:3], to_end[:, 0:1]), q["ends"])
            dve.wait_ge(q["pool_const"], 1)
            dve.wait_ge(q["blk_all"], 1)
            for k in range(TN):
                v.tensor_scalar(wgb[k][:, 0:R], banks[0][0:R, 0:R], thr[:, k:k + 1], 0.0, ALU.is_lt, ALU.add,
                                accum_out=blk_f[:, k:k + 1])
            after(v.memset(carry_row[:, :, :], 0.0), st)
            after(v.tensor_copy(blk_u[:, :], blk_f[:, :]), q["blk_idx"])
            weight_low(0)
            dve.wait_ge(q["ends_in"], 16)
            v.tensor_tensor_scan(scan_row[:, 0, :], run_row[:, 1, :], run_row[:, 0, :], 0.0, ALU.mult, ALU.add)
            after(v.tensor_tensor_scan(scan_row[:, 1, ::-1], run_row[:, 3, ::-1], run_row[:, 2, ::-1], 0.0,
                                       ALU.mult, ALU.add), st)
            v.tensor_copy(carry_row[:, 0, 1:R], scan_row[:, 0, 0:R - 1])
            after(v.tensor_copy(carry_row[:, 1, 0:R - 1], scan_row[:, 1, 1:R]), q["carries"])
            dve.wait_ge(q["bias_ld"], 16 * 6)
            v.tensor_copy(ones_r[:, :], ones[0:2, :])
            after(v.tensor_copy(bias_hi[:, :, :], bias_in[:, :, :]), st)
            after(v.tensor_tensor(bias_h[:, :, :], bias_in[:, :, :], bias_hi[:, :, :].bitcast(fp32), ALU.subtract), st)
            after(v.tensor_scalar(bias_h[:, :, :], bias_h[:, :, :], ident[0:2, 1:2], None, ALU.mult), st)
            after(v.scalar_tensor_tensor(bias_r[:, :, :], bias_hi[:, :, :].bitcast(fp32), ident[0:2, 0:1], bias_h[:, :, :],
                                         ALU.mult, ALU.add), st)
            for n in range(1, len(convs)):
                weight_low(n)
            dve.wait_ge(q["carry_ld"], 16)
            v.tensor_tensor_scan(from_start, before, one, carry_in[:, 0:1], ALU.mult, ALU.add)
            after(v.tensor_tensor_scan(to_end[:, ::-1], behind[:, ::-1], one, carry_in[:, 1:2], ALU.mult, ALU.add), st)
            after(v.scalar_tensor_tensor(deg, from_start, -1.0, to_end, ALU.add, ALU.add), st)
            v.reciprocal(stat[:, :, 2], deg)
            v.tensor_copy(stat[:, :, 1], dst_f)
            v.memset(stat[:, :, 3], 0.0)
            dve.wait_ge(q["src_in"], 16)
            after(v.tensor_copy(stat[:, :, 0].bitcast(i32), src_i), q["rec_done"])
            dve.wait_ge(q["row_in"], 16 * TN)
            for k in range(TN):
                v.tensor_scalar(wgb[k], wg[k].bitcast(i32), thr[:, k:k + 1], 0.0, ALU.is_lt, ALU.add,
                                accum_out=blk_cnt[:, k:k + 1])
            after(v.tensor_copy(lane_cnt[:, :], ones[0:R, 0:1]), st)
            after(v.scalar_tensor_tensor(lo_f[:, :], blk_f[:, :], float(EB), blk_cnt[:, :], ALU.mult, ALU.add), st)
            after(v.tensor_copy(lo_i[:, :], lo_f[:, :]), q["lo_done"])
            weight_low(len(convs))
            dve.wait_ge(q["lo_in"], 16)
            flag, first, number, chunk_f, listed, until, key = (t[:, :] for t in grp)
            v.memset(bound[:, NT:NT + 1], float(E))
            v.tensor_copy(bound[:, 0:NT], lo_row[:, :])
            after(v.tensor_reduce(ordered[:, :], run_row[:, 4, :], AX.X, ALU.min), st)
            v.tensor_tensor(tile_cnt[:, :], bound[:, 1:NT + 1], bound[:, 0:NT], ALU.subtract)
            v.tensor_tensor(number, bound[:, TE:NT + 1:TE], bound[:, 0:NT:TE], ALU.subtract)
            v.tensor_scalar(first, bound[:, 0:NT:TE], ordered[:, 0:1], None, ALU.mult)
            after(v.tensor_scalar(unordered[:, :], ordered[:, :], -1.0, 1.0, ALU.mult, ALU.add), st)
            v.tensor_reduce(listed, tile_cnt[:, :].rearrange("p (g k) -> p g k", k=TE), AX.X, ALU.max)
            v.tensor_copy(fix_start[:, :], first)
            after(v.tensor_scalar(all_edges[:, :], unordered[:, :], float(E), None, ALU.mult), st)
            v.tensor_scalar(flag, listed, float(EC), unordered[:, 0:1], ALU.is_gt, ALU.max)
            after(v.tensor_scalar(chunk_f, number, ordered[:, 0:1], all_edges[:, 0:1], ALU.mult, ALU.add), st)
            after(v.tensor_scalar(number, chunk_f, float(EC - 1), None, ALU.add), st)
            after(v.tensor_copy(fix_before[:, :], number), st)
            after(v.tensor_scalar(fix_chunks[:, :], fix_before[:, :], EC.bit_length() - 1, None, ALU.logical_shift_right), st)
            after(v.tensor_copy(chunk_f, fix_chunks[:, :]), st)
            v.tensor_reduce(fix_sum[:, :], flag, AX.X, ALU.add)
            v.tensor_tensor_scan(key, ones[0:1, 0:NG], flag, 0.0, ALU.mult, ALU.add)
            after(v.tensor_tensor(listed, chunk_f, flag, ALU.mult), st)
            v.tensor_tensor_scan(until, ones[0:1, 0:NG], listed, 0.0, ALU.mult, ALU.add)
            after(v.tensor_tensor(place[:, :], key, flag, ALU.mult), q["place"])
            v.tensor_tensor(number, until, listed, ALU.subtract)
            dve.wait_ge(q["listed"], 1)
            after(v.tensor_copy(place_col[:, :], banks[1][0:NG, 0:1]), st)
            after(v.tensor_scalar(place_at, iota_n[0:NG, 1:NG + 1], place_col[:, 0:1], None, ALU.is_equal), q["place"])
            v.tensor_copy(fix_before[:, :], number)
            v.tensor_copy(fix_num[:, :], fix_sum[:, :])
            dve.wait_ge(q["listed"], 2)
            after(v.tensor_scalar(fix_list[:, :], banks[2][0:1, 0:NG], float(-N), 0.0, ALU.add, ALU.max), st)
            dve.sem_inc(q["fix_ok"], 1)
            for f in (fa, fb):
                dve.sem_inc(f["free"], 1)
            weight_low(len(convs) + 1)

            def low_parts(g, s, e, blocks):
                for n in blocks:
                    own, d, bank = operand(e, n)
                    hi, lo = (XTH, XTL) if own else (ATH, ATL)
                    dve.wait_ge(e["hi"], 2 * KD * g + n + 1)
                    v.tensor_tensor(lo[:, s, d, :], banks[bank][:, 0:GN], hi[:, s, d, :].bitcast(fp32),
                                    ALU.subtract).then_inc(e["lo"], 1)

            def edge_ends(g, s, e, first):
                if not first:
                    dve.wait_ge(e["A"], KD * (g - 1))
                v.scalar_tensor_tensor(S[:, s], iota_n[:, :].rearrange("p (j n) -> p j n", j=TE), tile_base[:, ds(TE * g, 1)],
                                       edge_tab[:, ds(TE * g, TE), 1:2].broadcast_to([P, TE, NE]),
                                       ALU.add, ALU.is_equal).then_inc(e["S"], 1)

            def stats_a(g, s, turn):
                dve.wait_ge(a[f"x{s}"], 16 * (turn + 1))
                for k in range(TN):
                    v.bn_stats(ST[0:R, s, k, :], X[0:R, s, k, :])
                dve.wait_ge(a[f"ga{s}"], 16 * TE * (turn + 1))
                for j in range(TE):
                    last = v.bn_stats(ST[:, s, TN + j, :], G[:, s, j, :])
                last.then_inc(a["stats"], 1)
                dve.wait_ge(a["stats"], g + 1)
                v.memset(dve_scrap[:, :], 0.0)
                for k in range(TN + TE):
                    rows = R if k < TN else P
                    last = v.bn_aggr(MV[0:rows, s, k, :], ST[0:rows, s, k, :])
                last.then_inc(a["aggr"], 1)

            def rstd_a(g, s):
                dve.wait_ge(a["sqrt"], g + 1)
                v.reciprocal(RR[:, s, :], RT[:, s, :]).then_inc(a["rstd"], 1)
                dve.wait_ge(a["rstd"], g + 1)
                v.scalar_tensor_tensor(NMR[:, s, :], MV[:, s, :, 0], -1.0, RR[:, s, :], ALU.mult, ALU.mult).then_inc(a["nmr"], 1)
                number = edge_tab[:, ds(TE * g, TE), 2]
                v.tensor_tensor(RP[:, s, TN:], RR[:, s, TN:], number, ALU.mult)
                dve.wait_ge(a["nmr"], g + 1)
                v.tensor_tensor(NMR[:, s, TN:], NMR[:, s, TN:], number, ALU.mult).then_inc(a["nme"], 1)

            def turn_a(g, s, turn, first=False):
                edge_ends(g + 1, 1 - s, a, first)
                rstd_a(g + 1, 1 - s)
                low_parts(g, s, a, range(2 * KD))
                stats_a(g + 2, s, turn + 1)

            stats_a(0, 0, 0)
            rstd_a(0, 0)
            edge_ends(0, 0, a, True)
            stats_a(1, 1, 0)
            turn_a(0, 0, 0, True)
            turn_a(1, 1, 0)
            with dve.Fori(1, NG // 2 - 1) as i:
                turn_a(2 * i, 0, i)
                turn_a(2 * i + 1, 1, i)
            low_parts(NG - 2, 0, a, range(KD))
            rstd_a(NG - 1, 1)
            edge_ends(NG - 1, 1, a, False)
            low_parts(NG - 2, 0, a, range(KD, 2 * KD))
            low_parts(NG - 1, 1, a, range(2 * KD))

            def counted(on, base, per):
                n = [0]

                def step_(ins):
                    n[0] += 1
                    assert n[0] <= per
                    ins.then_inc(on, 1)
                    dve.wait_ge(on, base + n[0])
                    dve.sem_inc(q["waited"], 1)
                return step_, n

            def repair(f, second):
                CHUNK_STEPS, ROW_STEPS = (4 if second else 7), (21 if second else 13)
                dve.wait_ge(q["fix_ok"], 1)
                num = dve.value_load(fix_num[0:1, 0:1], min_val=0, max_val=NG)
                with dve.If(num > 0):
                    with dve.Fori(0, num) as k:
                        g = dve.value_load(fix_list[0:1, ds(k, 1)], min_val=0, max_val=NG - 1)
                        chunks = dve.value_load(fix_chunks[0:1, ds(g, 1)], min_val=1, max_val=CH_MAX)
                        before = dve.value_load(fix_before[0:1, ds(g, 1)], min_val=0, max_val=NG * CH_MAX)
                        step_, rows_n = counted(f["row_step"], ROW_STEPS * k, ROW_STEPS)
                        step_(v.memset(fix_sums[:, :, :], 0.0))
                        with dve.Fori(0, chunks) as j:
                            chunk, n = counted(f["step"], CHUNK_STEPS * (before + j), CHUNK_STEPS)
                            dve.wait_ge(f["in"], before + j + 1)
                            dve.sem_inc(q["waited"], 1)
                            if not second:
                                chunk(v.bn_stats(ST[:, 0, 0, :], G[:, 0, 0, :]))
                                v.bn_aggr(MV[:, 0, 0, :], ST[:, 0, 0, :]).then_inc(f["aggr"], 1)
                                dve.wait_ge(f["sqrt"], before + j + 1)
                                chunk(v.reciprocal(RR[:, 0, 0:1], RT[:, 0, 0:1]))
                                chunk(v.tensor_scalar(GB[:, 0, 0, :], G[:, 0, 0, :], MV[:, 0, 0, 0:1], RR[:, 0, 0:1],
                                                      ALU.subtract, ALU.mult))
                            chunk(v.tensor_tensor(edge_at[:, 0, 0:1], fix_rec[:, 1:2], tile_base[:, ds(TE * g, 1)], ALU.subtract))
                            v.tensor_scalar(S[:, 0].rearrange("p k n -> p (k n)"), iota_n[:, :], edge_at[:, 0, 0:1], None,
                                            ALU.is_equal).then_inc(f["op"], 1)
                            dve.wait_ge(f["sums"], before + j + 1)
                            for d in range(KD + 1):
                                chunk(v.tensor_tensor(fix_sums[:, d, :], fix_sums[:, d, :], banks[KD + d][:, 0:GN], ALU.add))
                            dve.sem_inc(f["free"], 1)
                            assert n[0] == CHUNK_STEPS
                        step_(v.tensor_scalar(fix_sums[:, KD, :], fix_sums[:, KD, :], 1.0, None, ALU.max))
                        step_(v.reciprocal(fix_sums[:, KD, :], fix_sums[:, KD, :]))
                        for d in range(KD):
                            step_(v.tensor_tensor(fix_sums[:, d, :], fix_sums[:, d, :], fix_sums[:, KD, :], ALU.mult))
                        step_(v.tensor_copy(ATH[:, 0], fix_sums[:, 0:KD, :]))
                        step_(v.tensor_tensor(ATL[:, 0], fix_sums[:, 0:KD, :], ATH[:, 0].bitcast(fp32), ALU.subtract))
                        dve.wait_ge(f["rows"], 32 * k + 32)
                        dve.sem_inc(q["waited"], 1)

                        def stats(aggr_done, sqrt_done, count):
                            for m in range(TN):
                                last = v.bn_stats(ST[0:R, 0, m, :], X[0:R, 0, m, :])
                            step_(last)
                            for m in range(TN):
                                last = v.bn_aggr(MV[0:R, 0, m, :], ST[0:R, 0, m, :])
                            last.then_inc(aggr_done, 1)
                            dve.wait_ge(sqrt_done, count)
                            step_(v.reciprocal(RR[0:R, 0, 0:TN], RT[0:R, 0, 0:TN]))

                        if not second:
                            stats(f["row_aggr"], f["row_sqrt"], k + 1)
                            for m in range(TN):
                                last = v.tensor_scalar(XN[0:R, 0, m, :], X[0:R, 0, m, :], MV[0:R, 0, m, 0:1], RR[0:R, 0, m:m + 1],
                                                       ALU.subtract, ALU.mult)
                            last.then_inc(f["row_in"], 1)
                        else:
                            dve.sem_inc(f["row_in"], 1)
                        dve.wait_ge(f["T"], KD * k + KD)
                        for d in range(KD):
                            last = v.tensor_copy(XTH[:, 0, d, :], banks[d][:, 0:GN])
                        step_(last)
                        for d in range(KD):
                            last = v.tensor_tensor(XTL[:, 0, d, :], banks[d][:, 0:GN], XTH[:, 0, d, :].bitcast(fp32), ALU.subtract)
                        last.then_inc(f["lo"], 1)
                        dve.wait_ge(f["D"], k + 1)
                        for m in range(TN // 2):
                            rows = (X[0:R, 0] if second else O[:, 0])[:, 2 * m:2 * m + 2, :].rearrange("p k d -> p (k d)")
                            if second:
                                last = v.tensor_tensor(rows, banks[4 + m][0:R, :], rows, ALU.add)
                            else:
                                last = v.tensor_scalar(rows, banks[4 + m][0:R, :], 0.0, None, ALU.max)
                        if not second:
                            last.then_inc(f["res"], 1)
                        else:
                            step_(last)
                            stats(f["row_aggr"], f["row_sqrt"], k + 1)
                            router_rows(g, 0, step_)
                            for m in range(TN):
                                last = v.tensor_scalar(O[:, 0, m, :], X[0:R, 0, m, :], RP[0:R, 0, m:m + 1], NMR[0:R, 0, m:m + 1],
                                                       ALU.mult, ALU.add)
                            last.then_inc(f["res"], 1)
                        dve.wait_ge(f["landed"], k + 1)
                        for _ in range(ROW_STEPS - rows_n[0]):
                            step_(v.memset(dve_scrap[:, :], 0.0))

            def x1_b(g, s, turn):
                dve.wait_ge(b["D"], g + 1)
                dve.wait_ge(b[f"x{s}"], 16 * (turn + 1))
                for m in range(TN // 2):
                    rows = X[0:R, s, 2 * m:2 * m + 2, :].rearrange("p k d -> p (k d)")
                    last = v.tensor_tensor(rows, banks[4 + 2 * s + m][0:R, :], rows, ALU.add)
                last.then_inc(b["x1s"], 1)
                dve.wait_ge(b["x1s"], g + 1)
                for k in range(TN):
                    last = v.bn_stats(ST[0:R, s, k, :], X[0:R, s, k, :])
                last.then_inc(b["stats"], 1)
                dve.wait_ge(b["stats"], g + 1)
                v.memset(dve_scrap[:, :], 0.0)
                for k in range(TN):
                    last = v.bn_aggr(MV[0:R, s, k, :], ST[0:R, s, k, :])
                last.then_inc(b["aggr"], 1)

            def dots(s):
                for k in range(TN):
                    last = v.scalar_tensor_tensor(G[0:R, s, k, :], X[0:R, s, k, :], MV[0:R, s, k, 0:1], wr_row[:, :],
                                                  ALU.subtract, ALU.mult, accum_out=wdot[:, s, k:k + 1])
                return last

            def router_rows(g, s, then):
                v.tensor_scalar(RP[0:R, s, 0:TN], RR[0:R, s, 0:TN], 1.0, None, ALU.add)
                v.scalar_tensor_tensor(NMR[0:R, s, 0:TN], MV[0:R, s, 0:TN, 0], -1.0, RR[0:R, s, 0:TN], ALU.mult, ALU.mult)
                then(dots(s))
                then(v.tensor_tensor(wdot[:, s, :], wdot[:, s, :], RR[0:R, s, 0:TN], ALU.mult))
                v.tensor_copy(stat[:, ds(TN * g, TN), 0], MV[0:R, s, 0:TN, 0])
                v.tensor_copy(stat[:, ds(TN * g, TN), 1], RR[0:R, s, 0:TN])
                then(v.tensor_scalar(stat[:, ds(TN * g, TN), 2], wdot[:, s, :], br_col[:, 0:1], None, ALU.add))

            def router_b(g, s, ends=True):
                dve.wait_ge(b["sqrt"], g + 1)
                v.reciprocal(RR[0:R, s, 0:TN], RT[0:R, s, 0:TN]).then_inc(b["rstd"], 1)
                dve.wait_ge(b["rstd"], g + 1)
                v.tensor_scalar(RP[0:R, s, 0:TN], RR[0:R, s, 0:TN], 1.0, None, ALU.add)
                v.scalar_tensor_tensor(NMR[0:R, s, 0:TN], MV[0:R, s, 0:TN, 0], -1.0, RR[0:R, s, 0:TN],
                                       ALU.mult, ALU.mult).then_inc(b["nmr"], 1)
                dots(s).then_inc(b["dot"], 1)
                if ends:
                    edge_ends(g + 4, s, b, False)
                dve.wait_ge(b["dot"], g + 1)
                v.tensor_tensor(wdot[:, s, :], wdot[:, s, :], RR[0:R, s, 0:TN], ALU.mult).then_inc(b["prod"], 1)
                v.tensor_copy(stat[:, ds(TN * g, TN), 0], MV[0:R, s, 0:TN, 0])
                v.tensor_copy(stat[:, ds(TN * g, TN), 1], RR[0:R, s, 0:TN])
                dve.wait_ge(b["prod"], g + 1)
                v.tensor_scalar(stat[:, ds(TN * g, TN), 2], wdot[:, s, :], br_col[:, 0:1], None, ALU.add).then_inc(b["tab"], 1)

            def turn_b(g, s, turn, first, last=False):
                low_parts(g, s, b, range(KD))
                if not first:
                    x1_b(g - 2, s, turn - 1)
                low_parts(g, s, b, range(KD, 2 * KD))
                if first:
                    edge_ends(g + 2, s, b, False)
                else:
                    router_b(g - 2, s, not last)

            repair(fa, False)
            dve.wait_ge(fa["done"], 1)
            edge_ends(0, 0, b, True)
            edge_ends(1, 1, b, True)
            turn_b(0, 0, 0, True)
            turn_b(1, 1, 0, True)
            with dve.Fori(0, NG // 4 - 1) as i:
                for n in range(4):
                    turn_b(4 * i + n + 2, n % 2, 2 * i + 1 + n // 2, False)
            turn_b(NG - 2, 0, NG // 2 - 1, False, True)
            turn_b(NG - 1, 1, NG // 2 - 1, False, True)
            for s in range(2):
                x1_b(NG - 2 + s, s, NG // 2 - 1)
                router_b(NG - 2 + s, s, False)
            dve.wait_ge(b["base"], NG)
            repair(fb, True)
            dve.wait_ge(fb["done"], 1)

            dve.wait_ge(b["tab"], NG)
            cs = c["step"]
            hi, lo, above, equal, flip, bits = wxn[0], wxn[1], wxn[2], wxn[3], wxn[4].bitcast(i32), wgb[0].bitcast(i32)
            half_i, strict, ties, scrap, key, rank = wgb[1].bitcast(i32), wgb[2], wgb[3], wgb[4], wgb[5], wg[0]
            col_sum, upto = wg[1], wg[2]
            place_in_lane, all_keys, over_key = wgb[1], wgb[4], wg[5]
            w_bits = stat[:, :, 2].bitcast(i32)
            after(v.tensor_scalar(flip, w_bits, 31, -2 ** 31, ALU.arith_shift_right, ALU.bitwise_or), cs)
            after(v.tensor_tensor(bits, flip, w_bits, ALU.bitwise_xor), cs)
            after(v.tensor_scalar(half_i, bits, 16, None, ALU.logical_shift_right), cs)
            after(v.tensor_copy(hi, half_i), cs)
            after(v.tensor_scalar(half_i, bits, 2 ** HALF_BITS - 1, None, ALU.bitwise_and), cs)
            after(v.tensor_copy(lo, half_i), cs)
            after(v.tensor_scalar(scrap, stat[:, :, 1], 1.0, None, ALU.add), cs)
            after(v.reciprocal(rank, scrap), cs)
            v.memset(stat[:, :, 3], 0.0)
            after(v.tensor_tensor(stat[:, :, 1], stat[:, :, 1], rank, ALU.mult), c["stat_done"])

            def search(data, level):
                v.memset(found[:, :], 0.0)
                v.tensor_scalar(steps[0][:, :], iota_n[0:R, 1:4], float(4 ** (DIGITS - 1)), None, ALU.mult)
                after(v.tensor_scalar(trial[:, :], iota_n[0:R, 1:4], float(4 ** (DIGITS - 1)), None, ALU.mult), cs)
                with dve.Fori(0, DIGITS // 2) as i:
                    for m in range(2):
                        n = 2 * i + (DIGITS * level + m)
                        for j in range(3):
                            last = v.tensor_scalar(wg[3 + j], data, trial[:, j:j + 1], 0.0, ALU.is_ge, ALU.add,
                                                   accum_out=lane_cnt3[:, j:j + 1])
                        last.then_inc(c["counted"], 1)
                        v.tensor_scalar(steps[1 - m][:, :], steps[m][:, :], 0.25, None, ALU.mult)
                        dve.wait_ge(c["total"], n + 1)
                        v.tensor_scalar(reach[:, :], banks[0][0:R, 0:3], float(KSEL), 0.0, ALU.is_ge, ALU.add,
                                        accum_out=digit[:, :]).then_inc(c["cand"], 1)
                        dve.wait_ge(c["cand"], 3 * n + 1)
                        v.scalar_tensor_tensor(found[:, :], digit[:, :], steps[m][:, 0:1], found[:, :], ALU.mult,
                                               ALU.add).then_inc(c["cand"], 1)
                        dve.wait_ge(c["cand"], 3 * n + 2)
                        v.tensor_scalar(trial[:, :], steps[1 - m][:, :], found[:, 0:1], None, ALU.add).then_inc(c["cand"], 1)
                        dve.wait_ge(c["cand"], 3 * n + 3)

            search(hi, 0)
            v.tensor_scalar(above, hi, found[:, 0:1], None, ALU.is_gt)
            after(v.tensor_scalar(equal, hi, found[:, 0:1], None, ALU.is_equal), cs)
            after(v.scalar_tensor_tensor(rank, lo, 1.0, equal, ALU.add, ALU.mult), cs)
            after(v.scalar_tensor_tensor(upto, above, float(2 ** (HALF_BITS + 1)), rank, ALU.mult, ALU.add), cs)
            after(v.tensor_scalar(lo, upto, -1.0, None, ALU.add), cs)
            search(lo, 1)
            v.tensor_scalar(ties, lo, found[:, 0:1], None, ALU.is_equal)
            v.tensor_scalar(strict, lo, found[:, 0:1], 0.0, ALU.is_gt, ALU.add, accum_out=lane_cnt[:, :]).then_inc(c["counted"], 1)
            dve.wait_ge(c["total"], 2 * DIGITS + 1)
            v.tensor_copy(col_sum, banks[2][0:R, 0:NC])
            after(v.tensor_scalar(need[:, :], banks[0][0:R, 0:1], -1.0, float(KSEL), ALU.mult, ALU.add), cs)
            v.memset(scrap, 1.0)
            after(v.tensor_copy(rank, banks[1][0:R, 0:NC]), cs)
            after(v.tensor_tensor_scan(upto, scrap, col_sum, 0.0, ALU.mult, ALU.add), cs)
            after(v.tensor_tensor(upto, upto, col_sum, ALU.subtract), cs)
            after(v.tensor_tensor(rank, upto, rank, ALU.add), cs)
            after(v.scalar_tensor_tensor(scrap, rank, need[:, 0:1], ties, ALU.is_lt, ALU.mult), cs)
            v.memset(upto, 1.0)
            after(v.tensor_tensor(rank, strict, scrap, ALU.add), cs)
            after(v.tensor_tensor_scan(place_in_lane, upto, rank, 0.0, ALU.mult, ALU.add), cs)
            v.tensor_scalar(over_cnt[:, :], place_in_lane[:, NC - 1:NC], float(-MAIN), 0.0, ALU.add, ALU.max).then_inc(c["counted"], 1)
            after(v.tensor_tensor(all_keys, rank, col_rank[:, :], ALU.mult), cs)
            after(v.scalar_tensor_tensor(key, place_in_lane, MAIN + 0.5, all_keys, ALU.is_lt, ALU.mult), cs)
            after(v.tensor_tensor(over_key, all_keys, key, ALU.subtract), cs)

            def next_eight(m):
                v.max(m8[:, :], key).then_inc(c["max8"], 1)
                dve.wait_ge(c["max8"], 2 * m + 1)
                v.tensor_scalar(m8far[:, :], m8[:, :], 0.0, FAR, ALU.is_equal, ALU.mult)
                v.match_replace(key, m8[:, :], key, 0.0).then_inc(c["max8"], 1)
                dve.wait_ge(c["max8"], 2 * m + 2)
                v.tensor_scalar(n_tab[:, ds(OCT * m, OCT)], m8[:, :], float(-R), lane[:, 0:1], ALU.mult, ALU.add)
                v.scalar_tensor_tensor(q_tab[:, ds(OCT * m, OCT)], m8far[:, :], lane[:, 1:2], m8[:, :], ALU.add,
                                       ALU.subtract).then_inc(c["tab8"], 1)
                dve.wait_ge(c["tab8"], m + 1)

            def next_over(step):
                for m in range(OVER_OCTS):
                    at, done = slice(OCT * m, OCT * m + OCT), 3 * (OVER_OCTS * step + m)
                    v.max(m8[:, :], over_key).then_inc(c["over8"], 1)
                    dve.wait_ge(c["over8"], done + 1)
                    v.tensor_scalar(m8far[:, :], m8[:, :], 0.0, FAR, ALU.is_equal, ALU.mult)
                    v.match_replace(over_key, m8[:, :], over_key, 0.0).then_inc(c["over8"], 1)
                    dve.wait_ge(c["over8"], done + 2)
                    v.tensor_scalar(over_rows[:, at, 0], m8[:, :], float(-R), lane[:, 0:1], ALU.mult, ALU.add)
                    v.scalar_tensor_tensor(over_rows[:, at, 1], m8far[:, :], lane[:, 1:2], m8[:, :], ALU.add, ALU.subtract)
                    last = v.scalar_tensor_tensor(over_at[:, at], iota_n[0:R, at], over_first[:, 0:1], m8far[:, :], ALU.add, ALU.add)
                    last.then_inc(c["over8"], 1)
                    dve.wait_ge(c["over8"], done + 3)
                    dve.sem_inc(q["waited"], 1)
                v.tensor_scalar(over_first[:, :], over_first[:, :], float(OVER), None, ALU.add)

            def norm_c(n, s, turn, first):
                dve.wait_ge(c[f"g{s}"], 2 * 16 * TN * (turn + 1))
                if not first:
                    dve.wait_ge(c["T"], KD * (n - 1))
                for k in range(TN):
                    last = v.tensor_scalar(X2[:, s, k, :], BG[:, s, k, :], SG[:, s, k, 0:1], SG[:, s, k, 1:2],
                                           ALU.subtract, ALU.mult)
                last.then_inc(c["x2"], 1)

            def low_c(n):
                for d in range(KD):
                    dve.wait_ge(c["hiT"], KD * n + d + 1)
                    v.tensor_tensor(CTL[:, d, :], banks[d][:, 0:GN], CTH[:, d, :].bitcast(fp32), ALU.subtract).then_inc(c["loT"], 1)

            def hidden_c(n, first):
                for h in range(KH):
                    dve.wait_ge(c["gelu"], KH * n + h + 1)
                    if not first and h == 0:
                        dve.wait_ge(c["m2b"], n)
                    v.tensor_copy(HTH[:, h, :], GL[:, h % 2, :]).then_inc(c["hhi"], 1)
                    dve.wait_ge(c["hhi"], KH * n + h + 1)
                    v.tensor_tensor(HTL[:, h, :], GL[:, h % 2, :], HTH[:, h, :].bitcast(fp32), ALU.subtract).then_inc(c["hlo"], 1)

            def result_c(n, s, turn, first, m):
                dve.wait_ge(c["m2a" if m == 0 else "m2b"], n + 1)
                if not first and m == 0:
                    dve.wait_ge(c[f"sc{s}"], 16 * TN * turn)
                for k in (2 * m, 2 * m + 1):
                    last = v.scalar_tensor_tensor(YO[:, s, k, :], banks[6 + m][0:R, (k % 2) * D:(k % 2) * D + D],
                                                  SG[:, s, k, 2:3], BG[:, s, k, :], ALU.mult, ALU.add)
                last.then_inc(c["y"], 1)

            def turn_c(n, s, turn, first):
                hidden_c(n, first and s == 0)
                norm_c(n + 1, 1 - s, turn + s, first and s == 0)
                result_c(n, s, turn, first, 0)
                low_c(n + 1)
                result_c(n, s, turn, first, 1)

            next_eight(0)
            dve.wait_ge(c["total"], 2 * DIGITS + 2)
            v.tensor_reduce(lane_max[:, :], banks[7][0:1, 0:R], AX.X, ALU.max)
            v.tensor_copy(over_first[:, :], banks[7][0:R, P:P + 1])
            after(v.tensor_copy(oct_f[:, :], banks[7][0:1, P + 1:P + 2]), cs)
            v.tensor_scalar(rest_f[:, :], tile_base[0:1, 0:REST_OCTS * (R * OCT // NE):R * OCT // NE], oct_f[:, 0:1], 0.0,
                            ALU.is_lt, ALU.add, accum_out=need[0:1, :])
            after(v.tensor_scalar(steps_f[:, :], iota_n[0:1, 0:OVER * OVER_MAX:OVER], lane_max[:, 0:1], 0.0,
                                  ALU.is_lt, ALU.add, accum_out=over_f[:, :]), cs)
            v.tensor_scalar(over_n[:, :], over_f[:, :], 1.0, None, ALU.max)
            after(v.tensor_scalar(oct_n[:, :], need[0:1, :], 1.0, float(MAIN_OCTS), ALU.max, ALU.add), c["octs"])
            octs = dve.value_load(oct_n[0:1, 0:1], min_val=MAIN_OCTS + 1, max_val=MAIN_OCTS + REST_OCTS)
            overs = dve.value_load(over_n[0:1, 0:1], min_val=1, max_val=OVER_MAX)
            next_eight(1)
            norm_c(0, 0, 0, True)
            low_c(0)
            next_over(0)
            turn_c(0, 0, 0, True)
            with dve.If(overs > 1):
                with dve.Fori(1, overs) as i:
                    dve.wait_ge(c["over"], 16 * OVER * i)
                    dve.sem_inc(q["waited"], 1)
                    next_over(i)
            turn_c(1, 1, 0, True)
            with dve.Fori(1, MAIN_OCTS - 1) as i:
                next_eight(i + 1)
                turn_c(2 * i, 0, i, False)
                turn_c(2 * i + 1, 1, i, False)
            with dve.Fori(MAIN_OCTS - 1, octs) as i:
                turn_c(2 * i, 0, i, False)
                turn_c(2 * i + 1, 1, i, False)

        @block.scalar
        def _(act):
            s_ = nc.scalar

            def high_parts(g, s, e, first, blocks):
                for n in blocks:
                    own, d, bank = operand(e, n)
                    act.wait_ge(e["T" if own else "A"], KD * g + d + 1)
                    if not first and n == 0:
                        act.wait_ge(e["D"], g - 1)
                    s_.activation((XTH if own else ATH)[:, s, d, :], banks[bank][:, 0:GN], ACT.Copy).then_inc(e["hi"], 1)

            def sqrt_a(g, s):
                act.wait_ge(a["aggr"], g + 1)
                s_.activation(RT[:, s, :], MV[:, s, :, 1], ACT.Sqrt, bias=eps_col[:, 0:1]).then_inc(a["sqrt"], 1)

            def norm_rows(g, s, first):
                if not first:
                    act.wait_ge(a["T"], KD * (g - 1))
                for k in range(TN):
                    last = s_.activation(XN[0:R, s, k, :], X[0:R, s, k, :], ACT.Identity, bias=NMR[0:R, s, k:k + 1],
                                         scale=RR[0:R, s, k:k + 1])
                last.then_inc(a["xn"], 1)

            def norm_edges(g, s, first):
                act.wait_ge(a["nme"], g + 1)
                if not first:
                    act.wait_ge(a["A"], KD * (g - 1))
                for j in range(TE):
                    last = s_.activation(GB[:, s, j, :], G[:, s, j, :], ACT.Identity, bias=NMR[:, s, TN + j:TN + j + 1],
                                         scale=RP[:, s, TN + j:TN + j + 1])
                last.then_inc(a["gn"], 1)

            def relu_a(g, s, turn, first):
                act.wait_ge(a["D"], g + 1)
                if not first:
                    act.wait_ge(a[f"st{s}"], 16 * turn)
                for m in range(TN // 2):
                    last = s_.activation(O[:, s, 2 * m:2 * m + 2, :].rearrange("p k d -> p (k d)"),
                                         banks[4 + 2 * s + m][0:R, :], ACT.Relu)
                last.then_inc(a["h"], 1)

            def load_weight(n):
                w, k, at, _, _ = weights[n]
                if n >= len(convs):
                    act.wait_ge(q["w_lo"], n)
                act.dma_start(at.rearrange("p (k n) -> p k n", k=k), w.rearrange("(k p) n -> p k n", p=P)).then_inc(q["w_ld"], 16)

            for n in range(len(convs)):
                load_weight(n)
            for n, (_, _, at, hi, _) in enumerate(weights):
                if n >= len(convs):
                    load_weight(n)
                    act.wait_ge(q["w_ld"], 16 * (n + 1))
                else:
                    act.wait_ge(q["w_ld"], 16 * len(convs))
                s_.activation(hi[:, :, :].rearrange(flat), at, ACT.Copy).then_inc(q["w_hi"], 1)

            sqrt_a(0, 0)
            norm_edges(0, 0, True)
            norm_rows(0, 0, True)
            sqrt_a(1, 1)

            def turn_a(g, s, turn, stage):
                high_parts(g, s, a, stage < 2, range(2 * KD))
                norm_edges(g + 1, 1 - s, stage < 1)
                norm_rows(g + 1, 1 - s, stage < 1)
                if stage > 1:
                    relu_a(g - 2, s, turn - 1, stage < 4)
                sqrt_a(g + 2, s)

            for g in range(4):
                turn_a(g, g % 2, g // 2, g)
            with act.Fori(2, NG // 2 - 1) as i:
                turn_a(2 * i, 0, i, 4)
                turn_a(2 * i + 1, 1, i, 4)
            high_parts(NG - 2, 0, a, False, range(2 * KD))
            norm_edges(NG - 1, 1, False)
            norm_rows(NG - 1, 1, False)
            relu_a(NG - 4, 0, NG // 2 - 2, False)
            high_parts(NG - 1, 1, a, False, range(2 * KD))
            for g in range(NG - 3, NG):
                relu_a(g, g % 2, g // 2, False)

            def repair(f, second):
                act.wait_ge(q["fix_ok"], 1)
                num = act.value_load(fix_num[0:1, 0:1], min_val=0, max_val=NG)
                with act.If(num > 0):
                    with act.Fori(0, num) as k:
                        if not second:
                            g = act.value_load(fix_list[0:1, ds(k, 1)], min_val=0, max_val=NG - 1)
                            chunks = act.value_load(fix_chunks[0:1, ds(g, 1)], min_val=1, max_val=CH_MAX)
                            before = act.value_load(fix_before[0:1, ds(g, 1)], min_val=0, max_val=NG * CH_MAX)
                            with act.Fori(0, chunks) as j:
                                act.wait_ge(f["aggr"], before + j + 1)
                                s_.activation(RT[:, 0, 0:1], MV[:, 0, 0, 1:2], ACT.Sqrt, bias=eps_col[:, 0:1]).then_inc(f["sqrt"], 1)
                        act.wait_ge(f["row_aggr"], k + 1)
                        s_.activation(RT[0:R, 0, 0:TN], MV[0:R, 0, 0:TN, 1], ACT.Sqrt,
                                      bias=eps_col[0:R, 0:1]).then_inc(f["row_sqrt"], 1)
                act.wait_ge(f["done"], 1)

            def base_b(g, s, turn, first):
                act.wait_ge(b["aggr"], g + 1)
                s_.activation(RT[0:R, s, 0:TN], MV[0:R, s, 0:TN, 1], ACT.Sqrt, bias=eps_col[0:R, 0:1]).then_inc(b["sqrt"], 1)
                act.wait_ge(b["nmr"], g + 1)
                if not first:
                    act.wait_ge(b[f"st{s}"], 16 * turn)
                for k in range(TN):
                    last = s_.activation(O[:, s, k, :], X[0:R, s, k, :], ACT.Identity, bias=NMR[0:R, s, k:k + 1],
                                         scale=RP[0:R, s, k:k + 1])
                last.then_inc(b["base"], 1)

            def edge_weights(g, s):
                act.wait_ge(b["S"], g + 1)
                for j in range(TE):
                    last = s_.activation(S[:, s, j, :], S[:, s, j, :], ACT.Copy, scale=edge_tab[:, ds(TE * g + j, 1), 2])
                last.then_inc(b["Sw"], 1)

            def turn_b(g, s, turn, stage, last=False):
                high_parts(g, s, b, stage < 2, range(2 * KD))
                if not last:
                    edge_weights(g + 1, 1 - s)
                if stage > 1:
                    base_b(g - 2, s, turn - 1, stage < 4)

            repair(fa, False)
            edge_weights(0, 0)
            for g in range(4):
                turn_b(g, g % 2, g // 2, g)
            with act.Fori(2, NG // 2 - 1) as i:
                turn_b(2 * i, 0, i, 4)
                turn_b(2 * i + 1, 1, i, 4)
            turn_b(NG - 2, 0, NG // 2 - 1, 4)
            turn_b(NG - 1, 1, NG // 2 - 1, 4, True)
            for s in range(2):
                base_b(NG - 2 + s, s, NG // 2 - 1, False)
            repair(fb, True)

            act.wait_ge(c["octs"], 1)
            octs = act.value_load(oct_n[0:1, 0:1], min_val=MAIN_OCTS + 1, max_val=MAIN_OCTS + REST_OCTS)

            def high_c(n, first):
                for d in range(KD):
                    act.wait_ge(c["T"], KD * n + d + 1)
                    if not first and d == 0:
                        act.wait_ge(c["h1"], KH * n)
                    s_.activation(CTH[:, d, :], banks[d][:, 0:GN], ACT.Copy).then_inc(c["hiT"], 1)

            def turn_c(n, first):
                for h in range(KH):
                    act.wait_ge(c["h1"], KH * n + h + 1)
                    if not first or h >= 2:
                        act.wait_ge(c["hlo"], KH * n + h - 1)
                    s_.activation(GL[:, h % 2, :], banks[2 + h % 4][:, 0:GN], ACT.Gelu_apprx_tanh,
                                  bias=fb1_col[:, h:h + 1]).then_inc(c["gelu"], 1)
                high_c(n + 1, False)

            high_c(0, True)
            turn_c(0, True)
            turn_c(1, False)
            with act.Fori(1, octs) as i:
                turn_c(2 * i, False)
                turn_c(2 * i + 1, False)

        @block.tensor
        def _(pe):
            t = nc.tensor
            pe.wait_ge(q["blk_last_ok"], 1)
            pe.wait_ge(q["pool_const"], 1)
            t.matmul(banks[0][0:R, 0:R], ones[0:1, 0:R], blk_last[:, :], start=True, stop=True).then_inc(q["blk_all"], 1)
            pe.wait_ge(q["place"], 1)
            t.matmul(banks[1][0:NG, 0:1], place[:, :], ones[0:1, 0:1], start=True, stop=True).then_inc(q["listed"], 1)
            pe.wait_ge(q["place"], 2)
            t.matmul(banks[2][0:1, 0:NG], lane[0:NG, 0:1], place_at, start=True, stop=True).then_inc(q["listed"], 1)
            pe.wait_ge(q["w_lo"], len(convs))

            def three(o, lh, ll, rh, rl, last):
                t.matmul(o, lh, rh, start=False, stop=False)
                t.matmul(o, lh, rl, start=False, stop=False)
                return t.matmul(o, ll, rh, start=False, stop=last)

            def transposes(rows, done):
                for d in range(KD):
                    for k in range(TN):
                        last = t.transpose(banks[d][:, R * k:R * k + R], rows[0:R, k, P * d:P * d + P], ident[0:R, 0:R])
                    last.then_inc(done, 1)

            def neighbours(edges, s, done):
                for d in range(KD):
                    for j in range(TE):
                        last = t.matmul(banks[KD + d][:, NE * j:NE * j + NE], edges[:, j, P * d:P * d + P], S[:, s, j, :],
                                        start=True, stop=True)
                    last.then_inc(done, 1)

            def dense(s, bias, wl, wr_, done):
                for k in range(TN):
                    o = banks[4 + 2 * s + k // 2][0:R, (k % 2) * D:(k % 2) * D + D]
                    t.matmul(o, ones_r[:, 0:R], bias_r[:, bias, :], start=True, stop=False)
                    for d in range(KD):
                        at = slice(R * k, R * k + R)
                        three(o, XTH[:, s, d, at], XTL[:, s, d, at], w_hi[wr_][:, d, :], w_lo[wr_][:, d, :], False)
                        last = three(o, ATH[:, s, d, at], ATL[:, s, d, at], w_hi[wl][:, d, :], w_lo[wl][:, d, :], d == KD - 1)
                last.then_inc(done, 1)

            def inputs_a(g, s, first):
                pe.wait_ge(a["gn"], g + 1)
                pe.wait_ge(a["S"], g + 1)
                if not first:
                    pe.wait_ge(a["lo"], 2 * KD * g - KD)
                neighbours(GB[:, s], s, a["A"])
                pe.wait_ge(a["xn"], g + 1)
                if not first:
                    pe.wait_ge(a["lo"], 2 * KD * g)
                transposes(XN[:, s], a["T"])

            def outputs_a(g, s, first):
                pe.wait_ge(a["lo"], 2 * KD * (g + 1))
                if not first:
                    pe.wait_ge(a["h"], g - 1)
                dense(s, 0, "w1l", "w1r", a["D"])

            inputs_a(0, 0, True)
            for g in range(2):
                inputs_a(g + 1, (g + 1) % 2, False)
                outputs_a(g, g % 2, True)
            with pe.Fori(1, NG // 2 - 1) as i:
                for s in range(2):
                    inputs_a(2 * i + s + 1, 1 - s, False)
                    outputs_a(2 * i + s, s, False)
            inputs_a(NG - 1, 1, False)
            outputs_a(NG - 2, 0, False)
            outputs_a(NG - 1, 1, False)

            def inputs_b(g, s, turn, first):
                pe.wait_ge(b[f"h{s}"], 16 * (turn + 1))
                if not first:
                    pe.wait_ge(b["lo"], 2 * KD * g - KD)
                transposes(XN[:, s], b["T"])
                pe.wait_ge(b[f"ga{s}"], 16 * TE * (turn + 1))
                pe.wait_ge(b["Sw"], g + 1)
                if not first:
                    pe.wait_ge(b["lo"], 2 * KD * g)
                neighbours(GB[:, s], s, b["A"])

            def outputs_b(g, s, first):
                pe.wait_ge(b["lo"], 2 * KD * (g + 1))
                if not first:
                    pe.wait_ge(b["x1s"], g - 1)
                dense(s, 1, "w2l", "w2r", b["D"])

            def repair(f, second):
                pe.wait_ge(q["fix_ok"], 1)
                num = pe.value_load(fix_num[0:1, 0:1], min_val=0, max_val=NG)
                with pe.If(num > 0):
                    with pe.Fori(0, num) as k:
                        g = pe.value_load(fix_list[0:1, ds(k, 1)], min_val=0, max_val=NG - 1)
                        chunks = pe.value_load(fix_chunks[0:1, ds(g, 1)], min_val=1, max_val=CH_MAX)
                        before = pe.value_load(fix_before[0:1, ds(g, 1)], min_val=0, max_val=NG * CH_MAX)
                        with pe.Fori(0, chunks) as j:
                            pe.wait_ge(f["op"], before + j + 1)
                            for d in range(KD + 1):
                                rows = GB[:, 0, 0, P * d:P * d + P] if d < KD else ones[:, :]
                                last = t.matmul(banks[KD + d][:, 0:GN], rows, S[:, 0].rearrange("p k n -> p (k n)"),
                                                start=True, stop=True)
                            last.then_inc(f["sums"], 1)
                        pe.wait_ge(f["row_in"], k + 1)
                        transposes(XN[:, 0], f["T"])
                        pe.wait_ge(f["lo"], k + 1)
                        dense(0, int(second), "w2l" if second else "w1l", "w2r" if second else "w1r", f["D"])
                pe.wait_ge(f["done"], 1)

            pe.wait_ge(a["h"], NG)
            repair(fa, False)
            inputs_b(0, 0, 0, True)
            for g in range(2):
                inputs_b(g + 1, (g + 1) % 2, (g + 1) // 2, False)
                outputs_b(g, g % 2, True)
            with pe.Fori(1, NG // 2 - 1) as i:
                for s in range(2):
                    inputs_b(2 * i + s + 1, 1 - s, i + s, False)
                    outputs_b(2 * i + s, s, False)
            inputs_b(NG - 1, 1, NG // 2 - 1, False)
            outputs_b(NG - 2, 0, False)
            outputs_b(NG - 1, 1, False)

            pe.wait_ge(b["x1s"], NG)
            repair(fb, True)
            for level in range(2):
                with pe.Fori(0, DIGITS) as i:
                    pe.wait_ge(c["counted"], i + (DIGITS * level + 1))
                    t.matmul(banks[0][0:R, 0:3], ones[0:R, 0:R], lane_cnt3[:, :], start=True, stop=True).then_inc(c["total"], 1)
            ties = wgb[3]
            pe.wait_ge(c["counted"], 2 * DIGITS + 1)
            t.matmul(banks[0][0:R, 0:1], ones[0:R, 0:R], lane_cnt[:, :], start=True, stop=True)
            t.matmul(banks[1][0:R, 0:NC], tri[:, :], ties, start=True, stop=True)
            t.matmul(banks[2][0:R, 0:NC], ones[0:R, 0:R], ties, start=True, stop=True).then_inc(c["total"], 1)

            pe.wait_ge(c["counted"], 2 * DIGITS + 2)
            t.matmul(banks[7][0:1, 0:R], over_cnt[:, :], ident[0:R, 0:R], start=True, stop=True)
            t.matmul(banks[7][0:R, P:P + 1], tri[:, :], over_cnt[:, :], start=True, stop=True)
            t.matmul(banks[7][0:R, P + 1:P + 2], ones[0:R, 0:R], over_cnt[:, :], start=True, stop=True).then_inc(c["total"], 1)

            pe.wait_ge(q["w_lo"], len(weights))
            pe.wait_ge(c["octs"], 1)
            octs = pe.value_load(oct_n[0:1, 0:1], min_val=MAIN_OCTS + 1, max_val=MAIN_OCTS + REST_OCTS)

            def rows_c(n, s, first):
                pe.wait_ge(c["x2"], n + 1)
                if not first:
                    pe.wait_ge(c["loT"], KD * n)
                transposes(X2[:, s], c["T"])

            def turn_c(n, s, first):
                pe.wait_ge(c["loT"], KD * (n + 1))
                for h in range(KH):
                    if not first or h >= 4:
                        pe.wait_ge(c["gelu"], KH * n + h - 3)
                    o = banks[2 + h % 4][:, 0:GN]
                    for d in range(KD):
                        at = slice(P * h, P * h + P)
                        t.matmul(o, f1_hi[:, d, at], CTH[:, d, :], start=(d == 0), stop=False)
                        t.matmul(o, f1_hi[:, d, at], CTL[:, d, :], start=False, stop=False)
                        last = t.matmul(o, f1_lo[:, d, at], CTH[:, d, :], start=False, stop=(d == KD - 1))
                    last.then_inc(c["h1"], 1)
                for k in range(TN):
                    if k == TN - 1:
                        rows_c(n + 1, 1 - s, False)
                    if not first and k % 2 == 0:
                        pe.wait_ge(c["y"], 2 * n - 1 + k // 2)
                    o = banks[6 + k // 2][0:R, (k % 2) * D:(k % 2) * D + D]
                    t.matmul(o, ones_r[:, 0:R], bias_r[:, 2, :], start=True, stop=False)
                    for h in range(KH):
                        if k == 0:
                            pe.wait_ge(c["hlo"], KH * n + h + 1)
                        at = slice(R * k, R * k + R)
                        last = three(o, HTH[:, h, at], HTL[:, h, at], f2_hi[:, h, :], f2_lo[:, h, :], h == KH - 1)
                    if k % 2:
                        last.then_inc(c["m2a" if k == 1 else "m2b"], 1)

            rows_c(0, 0, True)
            turn_c(0, 0, True)
            turn_c(1, 1, False)
            with pe.Fori(1, octs) as i:
                for s in range(2):
                    turn_c(2 * i + s, s, False)


_INS = ["x", "src", "dst", "L0_gnn_W1_l", "L0_gnn_b1", "L0_gnn_W1_r", "L0_gnn_W2_l", "L0_gnn_b2", "L0_gnn_W2_r",
        "L0_ffn_wr", "L0_ffn_br", "L0_ffn_w1", "L0_ffn_b1", "L0_ffn_w2", "L0_ffn_b2"]


def kernel(**inputs):
    import numpy as np
    import concourse.bacc as bacc
    from concourse.bass_utils import run_bass_kernel_spmd

    nc = bacc.Bacc("TRN2", target_bir_lowering=False, num_devices=1)
    arrays, args = {}, []
    for name in _INS:
        a = np.ascontiguousarray(inputs[name])
        arrays["in_" + name] = a
        args.append(nc.dram_tensor("in_" + name, a.shape, mybir.dt.from_np(a.dtype), kind="ExternalInput").ap())
    n, d = inputs["x"].shape
    args.append(nc.dram_tensor("result", [n, d], mybir.dt.float32, kind="ExternalOutput").ap())
    gnn_ffn_kernel(nc, *args)
    r = run_bass_kernel_spmd(nc, [arrays], core_ids=[0])
    return r.results[0]["result"]
```
